# Optimizing a Trainium2 kernel written in Bass

```python
import numpy as np
import jax
import jax.numpy as jnp

def _softmax(x, axis=-1):
    return jax.nn.softmax(x, axis=axis)

def _gelu(x):
    return jax.nn.gelu(x, approximate=True)

def _silu(x):
    return jax.nn.silu(x)

def _sigmoid(x):
    return jax.nn.sigmoid(x)

def _layernorm(x, axis=-1, eps=1e-05):
    m = jnp.mean(x, axis=axis, keepdims=True)
    v = jnp.var(x, axis=axis, keepdims=True)
    return (x - m) / jnp.sqrt(v + eps)

def _scatter_add(tgt, idx, src, axis=0):
    return tgt.at[idx].add(src)

def _segment_sum(src, seg, n):
    return jax.ops.segment_sum(src, seg, n)
kernel_name = 'mk_adaln_d1_jaxref_r8_6333e3'

def setup_inputs(seed: int=0):
    np.random.seed(seed)
    _w = jnp.asarray

    def _L0_attn_setup():
        import jax, jax.numpy as jnp
        import numpy as np
        from jax import lax
        D_MODEL, D_INNER, D_STATE, D_CONV, DT_RANK = (128, 256, 16, 4, 64)
        B, L = (1, 256)

        def _reference_tuple_inner(x, W_in, conv_w, conv_b, W_x, W_dt, b_dt, A_log, D, W_out):
            b, l, dm = x.shape
            di, n = (A_log.shape[0], A_log.shape[1])
            x_and_res = x @ W_in
            xc, res = (x_and_res[..., :di], x_and_res[..., di:])
            k = conv_w.shape[1]
            xp = jnp.pad(xc, ((0, 0), (k - 1, 0), (0, 0)))
            xconv = conv_b
            for j in range(k):
                xconv = xconv + xp[:, j:j + l, :] * conv_w[:, j]
            xs = jax.nn.silu(xconv)
            x_dbl = xs @ W_x
            dt_r = x_dbl[..., :DT_RANK]
            Bm = x_dbl[..., DT_RANK:DT_RANK + n]
            Cm = x_dbl[..., DT_RANK + n:]
            dt = jax.nn.softplus(dt_r @ W_dt + b_dt)
            A = -jnp.exp(A_log)
            dA = jnp.exp(jnp.einsum('bld,dn->bldn', dt, A))
            dBx = jnp.einsum('bld,bln->bldn', dt, Bm) * xs[..., None]

            def step(h, inp):
                dA_t, dBx_t, C_t = inp
                h = dA_t * h + dBx_t
                y = jnp.einsum('bdn,bn->bd', h, C_t)
                return (h, y)
            h0 = jnp.zeros((b, di, n), x.dtype)
            hT, ys = lax.scan(step, h0, (dA.transpose(1, 0, 2, 3), dBx.transpose(1, 0, 2, 3), Cm.transpose(1, 0, 2)))
            y = ys.transpose(1, 0, 2) + xs * D
            y = y * jax.nn.silu(res)
            out = y @ W_out
            return (out, hT)
        key = jax.random.key(seed)
        ks = jax.random.split(key, 10)
        s = lambda d: 1.0 / np.sqrt(d)
        return {'x': jax.random.normal(ks[0], (B, L, D_MODEL), jnp.float32), 'W_in': jax.random.normal(ks[1], (D_MODEL, 2 * D_INNER), jnp.float32) * s(D_MODEL), 'conv_w': jax.random.normal(ks[2], (D_INNER, D_CONV), jnp.float32) * s(D_CONV), 'conv_b': jax.random.normal(ks[3], (D_INNER,), jnp.float32) * 0.01, 'W_x': jax.random.normal(ks[4], (D_INNER, DT_RANK + 2 * D_STATE), jnp.float32) * s(D_INNER), 'W_dt': jax.random.normal(ks[5], (DT_RANK, D_INNER), jnp.float32) * s(DT_RANK), 'b_dt': jax.random.normal(ks[6], (D_INNER,), jnp.float32) * 0.01, 'A_log': jnp.log(jnp.tile(jnp.arange(1.0, D_STATE + 1.0, dtype=jnp.float32), (D_INNER, 1))), 'D': jnp.ones((D_INNER,), jnp.float32), 'W_out': jax.random.normal(ks[7], (D_INNER, D_MODEL), jnp.float32) * s(D_INNER)}
    _L0_attn_in = _L0_attn_setup()

    def _L0_ffn_setup():
        import jax, jax.numpy as jnp
        import numpy as np
        B, T, DIM = (2, 256, 128)
        H, DH, E, K = (16, 64, 8, 2)
        key = jax.random.key(seed)
        ks = jax.random.split(key, 7)
        s = 0.02
        return {'x': jax.random.normal(ks[0], (B, T, DIM), jnp.float32), 'Wq': jax.random.normal(ks[1], (H, DH, DIM), jnp.float32) * s, 'Wk': jax.random.normal(ks[2], (H, DH, DIM), jnp.float32) * s, 'Wv': jax.random.normal(ks[3], (E, DH, DIM), jnp.float32) * s, 'Ws': jax.random.normal(ks[4], (H, E, DIM), jnp.float32) * s, 'Wd': jax.random.normal(ks[5], (H, E, DIM), jnp.float32) * s, 'Wo': jax.random.normal(ks[6], (E, DIM, DH), jnp.float32) * s}
    _L0_ffn_in = _L0_ffn_setup()
    _L0_c = _w((lambda *s: np.random.randn(*s).astype(np.float32) * 0.05)(16, 128))
    _L0_wmod = _w((lambda *s: np.random.randn(*s).astype(np.float32) * 0.05)(128, 6 * 128) * 128 ** (-0.5))
    _d = {'L0_attn_x': _L0_attn_in['x'], 'L0_attn_W_in': _L0_attn_in['W_in'], 'L0_attn_conv_w': _L0_attn_in['conv_w'], 'L0_attn_conv_b': _L0_attn_in['conv_b'], 'L0_attn_W_x': _L0_attn_in['W_x'], 'L0_attn_W_dt': _L0_attn_in['W_dt'], 'L0_attn_b_dt': _L0_attn_in['b_dt'], 'L0_attn_A_log': _L0_attn_in['A_log'], 'L0_attn_D': _L0_attn_in['D'], 'L0_attn_W_out': _L0_attn_in['W_out'], 'L0_ffn_Wq': _L0_ffn_in['Wq'], 'L0_ffn_Wk': _L0_ffn_in['Wk'], 'L0_ffn_Wv': _L0_ffn_in['Wv'], 'L0_ffn_Ws': _L0_ffn_in['Ws'], 'L0_ffn_Wd': _L0_ffn_in['Wd'], 'L0_ffn_Wo': _L0_ffn_in['Wo'], 'L0_c': _L0_c, 'L0_wmod': _L0_wmod}
    _x0 = _d['L0_attn_x']
    _d['L0_attn_x'] = jax.random.normal(jax.random.fold_in(jax.random.key(seed), 1), (16, 256, 128), dtype=_x0.dtype)
    del _x0
    return _d

def reference(L0_attn_x, L0_attn_W_in, L0_attn_conv_w, L0_attn_conv_b, L0_attn_W_x, L0_attn_W_dt, L0_attn_b_dt, L0_attn_A_log, L0_attn_D, L0_attn_W_out, L0_ffn_Wq, L0_ffn_Wk, L0_ffn_Wv, L0_ffn_Ws, L0_ffn_Wd, L0_ffn_Wo, L0_c, L0_wmod):

    def _L0_attn_ref(x, W_in, conv_w, conv_b, W_x, W_dt, b_dt, A_log, D, W_out):
        import jax, jax.numpy as jnp
        import numpy as np
        from jax import lax
        D_MODEL, D_INNER, D_STATE, D_CONV, DT_RANK = (128, 256, 16, 4, 64)
        B, L = (1, 256)

        def _reference_tuple_inner(x, W_in, conv_w, conv_b, W_x, W_dt, b_dt, A_log, D, W_out):
            b, l, dm = x.shape
            di, n = (A_log.shape[0], A_log.shape[1])
            x_and_res = x @ W_in
            xc, res = (x_and_res[..., :di], x_and_res[..., di:])
            k = conv_w.shape[1]
            xp = jnp.pad(xc, ((0, 0), (k - 1, 0), (0, 0)))
            xconv = conv_b
            for j in range(k):
                xconv = xconv + xp[:, j:j + l, :] * conv_w[:, j]
            xs = jax.nn.silu(xconv)
            x_dbl = xs @ W_x
            dt_r = x_dbl[..., :DT_RANK]
            Bm = x_dbl[..., DT_RANK:DT_RANK + n]
            Cm = x_dbl[..., DT_RANK + n:]
            dt = jax.nn.softplus(dt_r @ W_dt + b_dt)
            A = -jnp.exp(A_log)
            dA = jnp.exp(jnp.einsum('bld,dn->bldn', dt, A))
            dBx = jnp.einsum('bld,bln->bldn', dt, Bm) * xs[..., None]

            def step(h, inp):
                dA_t, dBx_t, C_t = inp
                h = dA_t * h + dBx_t
                y = jnp.einsum('bdn,bn->bd', h, C_t)
                return (h, y)
            h0 = jnp.zeros((b, di, n), x.dtype)
            hT, ys = lax.scan(step, h0, (dA.transpose(1, 0, 2, 3), dBx.transpose(1, 0, 2, 3), Cm.transpose(1, 0, 2)))
            y = ys.transpose(1, 0, 2) + xs * D
            y = y * jax.nn.silu(res)
            out = y @ W_out
            return (out, hT)
        return _reference_tuple_inner(x, W_in, conv_w, conv_b, W_x, W_dt, b_dt, A_log, D, W_out)[0]

    def _L0_ffn_ref(x, Wq, Wk, Wv, Ws, Wd, Wo):
        import jax, jax.numpy as jnp
        import numpy as np
        B, T, DIM = (2, 256, 128)
        H, DH, E, K = (16, 64, 8, 2)
        scale = DH ** (-0.5)
        q = jnp.einsum('btc,hdc->bhtd', x, Wq)
        k = jnp.einsum('btc,hdc->bhtd', x, Wk)
        gate_v = jnp.einsum('btc,hec->bthe', x, Ws)
        w, sel = jax.lax.top_k(gate_v, K)
        wsig = jax.nn.sigmoid(w)
        oh = jax.nn.one_hot(sel, E, dtype=x.dtype)
        mix_v = jnp.einsum('bthk,bthke->bthe', wsig, oh)
        proj_v = jnp.einsum('btc,edc->bted', x, Wv)
        v = jnp.einsum('bthe,bted->bhtd', mix_v, proj_v)
        scores = jnp.einsum('bhid,bhjd->bhij', q * scale, k)
        probs = jax.nn.softmax(scores, axis=-1)
        attn = jnp.einsum('bhij,bhjd->bihd', probs, v)
        gate_o = jnp.einsum('btc,hec->bthe', x, Wd)
        _, sel_o = jax.lax.top_k(gate_o, K)
        mask_o = jax.nn.one_hot(sel_o, E, dtype=x.dtype).sum(axis=3)
        res = jnp.einsum('bthe,bthd,efd->bthf', mask_o, attn, Wo)
        return res.sum(axis=2)
    x = L0_attn_x
    mod = (_silu(L0_c) @ L0_wmod).reshape(L0_c.shape[0], 6, 1, -1)
    sa, ca, ga, sb, cb, gb = (mod[:, 0], mod[:, 1], mod[:, 2], mod[:, 3], mod[:, 4], mod[:, 5])
    ga = (2 * (ga >= 0) - 1) * jnp.maximum(jnp.abs(ga), 0.25)
    gb = (2 * (gb >= 0) - 1) * jnp.maximum(jnp.abs(gb), 0.25)
    h = _layernorm(x, axis=-1) * (1 + ca) + sa
    x = x + ga * _L0_attn_ref(h, L0_attn_W_in, L0_attn_conv_w, L0_attn_conv_b, L0_attn_W_x, L0_attn_W_dt, L0_attn_b_dt, L0_attn_A_log, L0_attn_D, L0_attn_W_out)
    h = _layernorm(x, axis=-1) * (1 + cb) + sb
    x = x + gb * _L0_ffn_ref(h, L0_ffn_Wq, L0_ffn_Wk, L0_ffn_Wv, L0_ffn_Ws, L0_ffn_Wd, L0_ffn_Wo)
    return x

_drawn_inputs = setup_inputs


def setup_inputs(seed=0):
    import zlib

    import numpy as np

    out = dict(_drawn_inputs(seed))
    spreads = {'L0_attn_D': (1.0, 0.6)}
    factors = {'L0_attn_conv_b': 8.0,
     'L0_attn_b_dt': 8.0,
     'L0_ffn_Wq': 8.0,
     'L0_ffn_Wk': 8.0,
     'L0_ffn_Wv': 8.0,
     'L0_ffn_Ws': 8.0,
     'L0_ffn_Wd': 8.0,
     'L0_ffn_Wo': 8.0}
    for name, (base, spread) in spreads.items():
        noise = np.random.default_rng([zlib.crc32(name.encode()), seed]).standard_normal(out[name].shape)
        drawn = base * np.exp(spread * noise) if base else spread * noise
        out[name] = jnp.asarray(drawn.astype(out[name].dtype))
    for name, factor in factors.items():
        out[name] = (out[name] * factor).astype(out[name].dtype)
    return out
```

```python
from contextlib import ExitStack

import concourse.bass as bass
import numpy as np
from concourse import mybir

F32 = mybir.dt.float32
BF16 = mybir.dt.bfloat16
ALU = mybir.AluOpType
ACT = mybir.ActivationFunctionType
AX = mybir.AxisListType

P = 128
NSEQ, L, DM = 16, 256, 128
DI, NS, NCONV, RK = 256, 16, 4, 64
H, DH, NE = 16, 64, 8
NP = NSEQ // 2
TP = 2 * L
NT = TP // P
HALF = DI // P
SLOTS = 2 * H
NCH = NS
EPS = 1e-5


def constants():
    p = np.arange(P)
    q, low = p // 32, p % 32
    ident = np.eye(P)
    mv = np.stack([(low // 16 == s) & (q == qq) & (low // 8 % 2 == b)
                   for s in range(2) for qq in range(4) for b in range(2)], 1)
    mo = np.stack([(low // 16 == b) & (q == qq) for b in range(2) for qq in range(4)], 1)
    thr = np.broadcast_to(6.0 - np.arange(NE), (P, NE))
    misc = np.broadcast_to([-0.5, 1.0], (P, 2))
    return np.concatenate([ident, mv, mo, thr, misc], 1).astype(np.float32)


class Signal:

    def __init__(self, sem, per):
        self.sem, self.per = sem, per

    def at(self, k, j):
        count = k * self.per + j
        return max(count, 0) if isinstance(count, int) else count


def grow(ap, axis, n):
    ap = ap.unsqueeze(axis)
    shape = list(ap.shape)
    shape[axis] = n
    return ap.to_broadcast(shape)


def build(nc, x, W_in, conv_w, conv_b, W_x, W_dt, b_dt, A_log, D, W_out, Wq, Wk, Wv, Ws, Wd, Wo, c_in, wmod, const, out):
    ctx = ExitStack()
    with ctx:
        def sb(name, shape, dt=F32):
            return ctx.enter_context(nc.sbuf_tensor(name, shape, dt))

        def sig(name, per=1):
            return Signal(ctx.enter_context(nc.semaphore("s_" + name)), per)

        bc_dram = nc.dram_tensor("bc_rows", [NP, 2 * NS, TP], F32).ap()
        x1_dram = nc.dram_tensor("x1_rows", [NP, P, NT, DM], F32).ap()
        gate_dram = nc.dram_tensor("gate_rows", [2, NSEQ, DM], F32).ap()

        cst = sb("cst", [P, P + 16 + 8 + 8 + 2])
        ident = cst[:, 0:128]
        mask_v = cst[:, 128:144]
        mask_o = cst[:, 144:152]
        thr = cst[:, 152:160]
        minus_half = cst[:, 160:161]
        one = cst[:, 161:162]
        w_in = sb("w_in", [P, 2 * DI])
        w_x = sb("w_x", [P, HALF, RK + 2 * NS])
        w_dt = sb("w_dt", [RK, DI])
        w_out = sb("w_out", [P, HALF, DM])
        cw = sb("cw", [P, HALF, NCONV])
        cb = sb("cb", [P, HALF])
        bdt = sb("bdt", [P, HALF])
        a_neg = sb("a_neg", [P, HALF, NS])
        d_skip = sb("d_skip", [P, HALF])
        m_qk = sb("m_qk", [P, H, DM])
        wv_t = sb("wv_t", [P, NE * DH])
        wg_t = sb("wg_t", [P, 2, NE, H])
        wo_t = sb("wo_t", [DH, NE, DM])
        mod_t = sb("mod_t", [P, 4, NSEQ])

        xa = sb("xa", [P, NT, DM])
        xn = sb("xn", [P, NT, DM])
        stat = sb("stat", [P, NT, 6])
        mv1 = sb("mv1", [P, NT, 2])
        ve1 = sb("ve1", [P, NT])
        rs1 = sb("rs1", [P, NT])
        cur1 = sb("cur1", [P, 2, 2])
        hT = sb("hT", [P, TP])
        xcp = sb("xcp", [P, HALF, 2, L + NCONV - 1])
        u = sb("u", [P, TP])
        thr_res = sb("thr_res", [P, TP])
        th_u = sb("th_u", [P, TP])
        sres1 = sb("sres1", [P, HALF, TP])
        sres2 = sb("sres2", [P, HALF, TP])
        xs = sb("xs", [P, HALF, TP])
        xdbl = sb("xdbl", [RK + 2 * NS, TP])
        lz = sb("lz", [P, HALF, TP])
        rz = sb("rz", [P, HALF, TP])
        dt2 = sb("dt2", [P, HALF, TP])
        dtx = sb("dtx", [P, HALF, TP])
        y = sb("y", [P, HALF, TP])
        dA = sb("dA", [P, 2, 2, 2, L])
        bx = sb("bx", [P, 3, 2, TP])
        Bb = sb("Bb", [P, 2, 2, TP])
        Cb = sb("Cb", [P, 2, 2, TP])
        xb = sb("xb", [P, NT, DM])
        ga = sb("ga", [P, 2, DM])
        x1 = sb("x1", [P, NT, DM])
        stat2 = sb("stat2", [P, NT, 6])
        mv2 = sb("mv2", [P, NT, 2])
        ve2 = sb("ve2", [P, NT])
        rs2 = sb("rs2", [P, NT])
        cur2 = sb("cur2", [P, 2, 2])
        hT2n = sb("hT2n", [P, TP])

        gall = rz[:, :, :].rearrange("p a t -> p (a t)").rearrange("p (e v n) -> p e v n", e=NE, v=2)
        thv = lz[:, 0, :].rearrange("p (e n) -> p e n", e=NE)
        mixn = lz[:, 1, :].rearrange("p (t e h) -> p t e h", t=NT, e=NE)
        beats = sb("beats", [P, NE - 1, P], BF16)
        score = sb("score", [P, NE, P], BF16)
        chosen = sb("chosen", [P, NE, 2, NT * H], BF16)
        mixT = sb("mixT", [P, 32, H])
        V2 = sb("V2", [P, 2, 32, DH])
        psb = V2[:, 0, :, :].rearrange("p r d -> p (r d)")
        P2 = sb("P2", [P, 32, DH])
        zT = P2[0:DH, :, :].rearrange("p r d -> p (r d)").rearrange("p (g r) -> p g r", r=32)
        bd = sb("bd", [P, 8, 16, H])
        bdo = bd[:, :, :, :].rearrange("p a c h -> p (a c h)").rearrange("p (r k e) -> p r k e", k=8, e=NE)
        v = sb("v", [P, 2, 32, DH])
        hT2 = sb("hT2", [P, TP])
        chosen_c = sb("chosen_c", [P, NE, NT * H], BF16)
        chosen_t = sb("chosen_t", [P, NE, 2 * H], BF16)
        qs = sb("qs", [P, 2, 2, L])
        nmax = sb("nmax", [P, 2, 2])
        Pm = sb("Pm", [P, 2, 2, L])
        PTs = sb("PTs", [P, 2, 2, L])
        lsum = sb("lsum", [P, 2, 2, H])
        attn = sb("attn", [P, 2, H, DH])
        rl = sb("rl", [P, 2 * H])
        mo = sb("mo", [P, NE, 2 * H])
        moT = sb("moT", [P, 32, NE])
        A2b = sb("A2b", [P, 32, DH])
        xr = sb("xr", [P, 2, DM])
        gb = sb("gb", [P, DM])
        ob = sb("ob", [P, 2, DM])

        wq_stage = V2[0:DH, :, :, :].rearrange("p s r d -> p (s r d)")[:, 0:H * DM].rearrange("p (h c) -> p h c", h=H)
        wk_stage = V2[0:DH, :, :, :].rearrange("p s r d -> p (s r d)")[:, H * DM:2 * H * DM].rearrange("p (h c) -> p h c", h=H)
        vst = v[:, :, :, :].rearrange("p s r d -> p (s r d)")
        wv_stage = vst[:, 0:512].rearrange("p (a c) -> p a c", a=4)
        ws_stage, wd_stage = vst[:, 512:640], vst[:, 640:768]
        wo_stage = vst[:, 768:1280].rearrange("p (e d) -> p e d", e=NE)
        wmod_stage = vst[:, 1280:2048]
        c_stage = vst[0:NSEQ, 2048:2176]
        cT, th_c, silu_c = vst[:, 2176:2192], vst[:, 2192:2208], vst[:, 2208:2224]
        g_raw, g_sign = vst[0:NSEQ, 2304:2560], vst[0:NSEQ, 2560:2816]
        g_abs = vst[0:NSEQ, 3072:3328]
        gate_rows = vst[0:NSEQ, 2816:3072].rearrange("n (g c) -> n g c", g=2)
        SETUP_DVE = 15

        def bank(name):
            return ctx.enter_context(nc.psum_tensor(name, [P, 512], F32))

        Y = [bank("Y0"), bank("Y1")]
        S = [bank("S0"), bank("S1")]
        Q, PT, O, X = bank("Q"), bank("PT"), bank("O"), bank("X")

        w_small = sig("w_small")
        su_pe, su_act, su_dve, su_gate, su_pool = sig("su_pe"), sig("su_act"), sig("su_dve"), sig("su_gate"), sig("su_pool")
        su_th = sig("su_th")
        s_xa, s_cur1, s_st1, s_mv1, s_ve1, s_rs1 = sig("xa", 16), sig("cur1"), sig("st1", 4), sig("mv1", 4), sig("ve1"), sig("rs1")
        s_xn, s_T1, s_hT, s_inp = sig("xn", 4), sig("T1"), sig("hT", 2), sig("inp", 4)
        s_xc, s_thr, s_sres, s_cv, s_thu, s_xs = sig("xc", 2), sig("thr", 2), sig("sres", 2), sig("cv", 8), sig("thu", 2), sig("xs", 2)
        s_xd, s_xds, s_bcw, s_zt, s_az, s_rz, s_ez, s_lz = (sig("xd"), sig("xds"), sig("bcw", 16), sig("zt", 2), sig("az", 2),
                                                           sig("rz", 2), sig("ez"), sig("lz"))
        s_dt, s_dtx, s_y0, s_sr2 = sig("dt"), sig("dtx"), sig("y0", 2), sig("sr2")
        s_bb = [sig("bb0", 64), sig("bb1", 64)]
        s_cb = [sig("cb0", 64), sig("cb1", 64)]
        s_dA, s_bm, s_scan, s_cm, s_ca, s_nr = (sig("dA", NCH), sig("bm", NCH), sig("scan", NCH), sig("cm", NCH), sig("ca", NCH),
                                                sig("nr", NCH))
        s_xb, s_ga, s_y1, s_y2, s_po, s_t1, s_x1, s_x1w = (sig("xb", 16), sig("ga", 16), sig("y1", 2), sig("y2"), sig("po"),
                                                           sig("t1"), sig("x1"), sig("x1w", 16))
        s_cur2, s_st2, s_mv2, s_ve2, s_rs2, s_xn2, s_T2, s_hTn = (sig("cur2"), sig("st2", 4), sig("mv2", 4), sig("ve2"),
                                                                  sig("rs2"), sig("xn2", 4), sig("T2"), sig("hTn", 2))
        s_gt, s_ga_sb, s_thv, s_score, s_chosen, s_sg, s_mix = (sig("gt", 2), sig("gall", 2), sig("thv"), sig("score", 22),
                                                                sig("chosen"), sig("sg"), sig("mix"))
        s_pp, s_ps, s_p2, s_mixT, s_bd, s_vm, s_v2 = (sig("pp", 4), sig("ps", 4), sig("p2"), sig("mixT"), sig("bd", 4),
                                                      sig("vm", 8), sig("v2", 8))
        s_v, s_hT2, s_cht, s_chc = sig("v", 2), sig("hT2"), sig("cht"), sig("chc")
        s_q, s_qs, s_sc, s_mx, s_ex, s_tp, s_pt, s_pv, s_oa = (sig("q", SLOTS // 2), sig("qs", SLOTS // 2), sig("sc", SLOTS), sig("mx", SLOTS),
                                                               sig("ex", SLOTS), sig("tp", SLOTS), sig("pt", SLOTS),
                                                               sig("pv", SLOTS), sig("oa", 8))
        s_xr, s_gb, s_rl, s_mo, s_moT, s_A2, s_bdo, s_z, s_zs, s_res, s_o1, s_ob, s_out = (
            sig("xr", 32), sig("gb", 32), sig("rl", 2), sig("mo", 2), sig("moT", 2), sig("A2", 2), sig("bdo", 2), sig("z", 8),
            sig("zs", 8), sig("res", 2), sig("o1", 2), sig("ob", 2), sig("out", 32))

        x_pairs = x.rearrange("(k s) (b t) c -> k t (s b) c", s=2, b=2)
        out_seqs = out.rearrange("n (b t) c -> n t b c", b=2)

        ENGINES = ("sync", "tensor", "scalar", "vector", "gpsimd")
        PLAN = {e: [] for e in ENGINES}

        def plan(time, *steps, **at):
            for step in steps:
                for e in ENGINES:
                    PLAN[e].append((at.get(e, time), step))

        plan(0.5, ("M2", "gate"))
        plan(1.0, ("M1", "start"))
        plan(1.5, ("M2", "project"))
        plan(2.5, ("M2", "residual"))
        plan(3.5, ("M2", "scale"))
        plan(4.0, ("A2b", "attn", 1))
        plan(4.5, ("A2b", "turn", 1), ("M2", "transpose"), scalar=5.0)
        plan(5.0, ("A2b", "spread", 1))
        for j in range(4):
            plan(6.5 + j, ("A2b", "z", 1, j), scalar=7.0 + j)
        plan(5.5, ("A0", "gates", 0), scalar=6.0)
        plan(6.0, ("A0", "gates", 1), scalar=6.5)
        plan(10.5, ("A2b", "out", 1))
        for d in range(1, NE):
            plan(6.5 + d / 2, ("A0", "rank", d))
        plan(10.5, ("A0", "top2"), scalar=7.0)
        for j in range(4):
            plan(7.0 + j, ("A0", "values", j), scalar=7.5 + j)
        plan(11.5, ("A0", "turn"))
        plan(12.0, ("A0", "spread", 0))
        for rc in range(4):
            t = 13.0 + 2 * rc
            plan(t, ("A0", "mix", rc, 0), scalar=t + 0.5)
            plan(t + 1, ("A0", "mix", rc, 1), scalar=t + 1.5)
            if rc < 3:
                plan(t + 1, ("A0", "spread", rc + 1))
        plan(16.0, ("M0", "norm"))
        plan(17.0, ("M0", "scale"))
        plan(18.5, ("M0", "transpose"), scalar=19.0)
        plan(18.0, ("A2a", "attn", 0))
        plan(19.0, ("A2a", "turn", 0))
        plan(20.5, ("A2a", "spread", 0))
        for j in range(4):
            plan(22.5 + j, ("A2a", "z", 0, j), scalar=23.0 + j)
            plan(21.0 + j, ("M0", "project", j), vector=21.5 + j)
        plan(27.0, ("A2a", "out", 0), vector=27.5)
        plan(24.0, ("M0", "conv", 0))
        plan(25.5, ("M0", "conv", 1))
        plan(27.5, ("M0", "xdbl"))
        plan(28.5, ("M0", "dt", 0))
        plan(29.5, ("M0", "dt", 1))
        plan(30.5, ("M0", "log"))
        for c in range(NCH):
            t = 1.5 + (14 * c) // 8
            plan(t, ("M1", "chunk", c), vector=t + 1)
            plan(t + 2, ("M1", "times_c", c))
            plan(t + 4 if c < NCH - 1 else 31.5, ("M1", "sum", c))
        for e in ENGINES:
            PLAN[e].sort(key=lambda entry: entry[0])

        def steps(engine, time):
            return [step for t, step in PLAN[engine] if t == time]

        LAG = {"M0": 1, "M1": 0, "M2": -1, "A0": -1, "A1": -2, "A2a": -2, "A2b": -3}
        FIRST, LAST = -1, NP + 2
        LOOP_FROM, LOOP_TO = 3, NP - 1

        def is_pair(k):
            return not isinstance(k, int) or 0 <= k < NP

        def has(stage, b):
            return is_pair(b + LAG[stage])

        def run(eng, body):
            for b in range(FIRST, LOOP_FROM):
                body(b)
            with eng.Fori(LOOP_FROM, LOOP_TO) as b:
                body(b)
            for b in range(LOOP_TO, LAST + 1):
                body(b)

        block = ctx.enter_context(nc.Block())

        @block.sync
        def _(sp):
            loads = [(cst[:, :], const), (w_in[:, :], W_in), (w_x[:, :, :], W_x.rearrange("(a p) n -> p a n", p=P)),
                     (w_dt[:, :], W_dt), (w_out[:, :, :], W_out.rearrange("(a p) n -> p a n", p=P)),
                     (cw[:, :, :], conv_w.rearrange("(a p) n -> p a n", p=P)),
                     (cb[:, :], conv_b.rearrange("(a p) -> p a", p=P)), (bdt[:, :], b_dt.rearrange("(a p) -> p a", p=P)),
                     (a_neg[:, :, :], A_log.rearrange("(a p) n -> p a n", p=P)),
                     (d_skip[:, :], D.rearrange("(a p) -> p a", p=P)),
                     (c_stage, c_in), (wmod_stage, wmod),
                     (wq_stage, Wq.rearrange("h d c -> d h c")), (wk_stage, Wk.rearrange("h d c -> d h c")),
                     (wv_stage, Wv.rearrange("(a e) d c -> (e d) a c", e=2)),
                     (ws_stage, Ws.rearrange("h e c -> (h e) c")), (wd_stage, Wd.rearrange("h e c -> (h e) c")),
                     (wo_stage, Wo.rearrange("e f d -> f e d"))]
            with nc.allow_non_contiguous_dma(reason="three vectors of 256 values, channels on partitions"):
                for dst, src in loads:
                    sp.dma_start(dst, src).then_inc(w_small.sem, 16)
            sp.wait_ge(su_gate.sem, su_gate.at(0, 1))
            sp.dma_start(gate_dram.rearrange("g n c -> n g c"), gate_rows).then_inc(su_pool.sem, 16)

            def step(k, stage, name, *a):
                if (stage, name) == ("M0", "norm"):
                    sp.wait_ge(s_xn.sem, s_xn.at(k, 0))
                    sp.dma_start(xa[:, :, :], x_pairs[k]).then_inc(s_xa.sem, 16)
                elif (stage, name) == ("M0", "xdbl"):
                    sp.wait_ge(s_xds.sem, s_xds.at(k, 1))
                    sp.dma_start(bc_dram[k], xdbl[RK:RK + 2 * NS, :]).then_inc(s_bcw.sem, 16)
                elif (stage, name) == ("M1", "chunk"):
                    if a[0] % 2 == 0:
                        g = a[0] // 2
                        rows = bc_dram[k, 2 * g:2 * g + 2, :]
                        if g == 0:
                            sp.wait_ge(s_dtx.sem, s_dtx.at(k, 1))
                        else:
                            sp.wait_ge(s_bm.sem, s_bm.at(k, 2 * (g - 1)))
                        sp.dma_start(Bb[:, g % 2], grow(rows, 0, P)).then_inc(s_bb[g % 2].sem, 16)
                        rows = bc_dram[k, NS + 2 * g:NS + 2 * g + 2, :]
                        sp.wait_ge(s_cm.sem, s_cm.at(k, 2 * (g - 1)))
                        sp.dma_start(Cb[:, g % 2], grow(rows, 0, P)).then_inc(s_cb[g % 2].sem, 16)
                elif (stage, name) == ("M2", "gate"):
                    if isinstance(k, int) and k == 0:
                        sp.wait_ge(su_pool.sem, su_pool.at(0, 16))
                    sp.wait_ge(s_x1w.sem, s_x1w.at(k, 0))
                    sp.dma_start(xb[:, :, :], x_pairs[k]).then_inc(s_xb.sem, 16)
                    sp.wait_ge(s_t1.sem, s_t1.at(k, 0))
                    sp.dma_start(ga[:, :, :], grow(gate_pairs[k], 0, P)).then_inc(s_ga.sem, 16)
                elif (stage, name) == ("M2", "residual"):
                    sp.wait_ge(s_x1.sem, s_x1.at(k, 1))
                    sp.dma_start(x1_dram[k], x1[:, :, :]).then_inc(s_x1w.sem, 16)
                elif name == "attn":
                    s = a[0]
                    if isinstance(k, int):
                        sp.wait_ge(s_x1w.sem, s_x1w.at(k, 16))
                    sp.wait_ge(s_ob.sem, s_ob.at(k, s))
                    sp.dma_start(xr[:, :, :], x1_dram[k, :, 2 * s:2 * s + 2, :]).then_inc(s_xr.sem, 16)
                    sp.wait_ge(s_o1.sem, s_o1.at(k, s))
                    sp.dma_start(gb[:, :], grow(gate_seqs[2 * k + s], 0, P)).then_inc(s_gb.sem, 16)
                elif name == "out":
                    s = a[0]
                    sp.wait_ge(s_ob.sem, s_ob.at(k, s + 1))
                    sp.dma_start(out_seqs[2 * k + s], ob[:, :, :]).then_inc(s_out.sem, 16)

            gate_pairs = gate_dram[0].rearrange("(k s) c -> k s c", s=2)
            gate_seqs = gate_dram[1]

            def body(b):
                for i in range(2 * SLOTS):
                    for stage, *a in steps("sync", i / 2):
                        if has(stage, b):
                            step(b + LAG[stage], stage, *a)

            run(sp, body)
            sp.wait_ge(s_out.sem, s_out.at(NP, 0))

        @block.tensor
        def _(pe):
            pe.wait_ge(w_small.sem, w_small.at(0, 16 * 18))

            nc.tensor.transpose(X[:, 0:NSEQ], c_stage, ident[0:NSEQ, 0:NSEQ]).then_inc(su_pe.sem, 1)
            pe.wait_ge(su_act.sem, su_act.at(0, 1))
            for i in range(4):
                last = nc.tensor.transpose(X[:, i * P:(i + 1) * P], wv_stage[:, i, :], ident)
            last.then_inc(su_pe.sem, 1)
            pe.wait_ge(su_act.sem, su_act.at(0, 2))
            nc.tensor.transpose(X[:, 0:P], ws_stage, ident)
            nc.tensor.transpose(X[:, P:2 * P], wd_stage, ident).then_inc(su_pe.sem, 1)
            for i in range(2):
                pe.wait_ge(su_act.sem, su_act.at(0, 3 + i))
                for j in range(4):
                    last = nc.tensor.transpose(X[0:DH, j * P:(j + 1) * P], wo_stage[:, 4 * i + j, :], ident)
                last.then_inc(su_pe.sem, 1)
            for i in range(4):
                pe.wait_ge(su_act.sem, su_act.at(0, 5 + i))
                for j in range(4):
                    last = nc.tensor.matmul(X[:, j * P:(j + 1) * P], wq_stage[:, 4 * i + j, :], wk_stage[:, 4 * i + j, :],
                                            start=True, stop=True)
                last.then_inc(su_pe.sem, 1)
            pe.wait_ge(su_dve.sem, su_dve.at(0, 1))
            pe.wait_ge(su_act.sem, su_act.at(0, 9))
            for i, part in enumerate((0, 1, 3, 4)):
                last = nc.tensor.matmul(X[:, i * NSEQ:(i + 1) * NSEQ], wmod_stage[:, part * DM:(part + 1) * DM], silu_c,
                                        start=True, stop=True)
            last.then_inc(su_pe.sem, 1)
            pe.wait_ge(su_act.sem, su_act.at(0, 10))
            for i, part in enumerate((2, 5)):
                last = nc.tensor.matmul(X[0:NSEQ, i * DM:(i + 1) * DM], silu_c, wmod_stage[:, part * DM:(part + 1) * DM],
                                        start=True, stop=True)
            last.then_inc(su_pe.sem, 1)
            pe.wait_ge(su_dve.sem, su_dve.at(0, SETUP_DVE))

            freed = [None]

            def fill(b, frees, lag, j):
                if freed[0] is not None:
                    s, lag0, j0 = freed[0]
                    pe.wait_ge(s.sem, s.at(b + lag0, j0))
                freed[0] = (frees, lag, j)

            def step(b, stage, name, *a):
                lag = LAG[stage]
                k = b + lag
                if (stage, name) == ("M0", "transpose"):
                    fill(b, s_hT, lag, 2)
                    pe.wait_ge(s_xn.sem, s_xn.at(k, 4))
                    for t in range(NT):
                        last = nc.tensor.transpose(X[:, t * P:(t + 1) * P], xn[:, t, :], ident)
                    last.then_inc(s_T1.sem, 1)
                elif (stage, name) == ("M0", "project"):
                    m = a[0]
                    fill(b, (s_xc if m < 2 else s_sres), lag, m % 2 + 1)
                    pe.wait_ge(s_hT.sem, s_hT.at(k, 2))
                    nc.tensor.matmul(X[:, :], w_in[:, m * P:(m + 1) * P], hT[:, :], start=True, stop=True).then_inc(s_inp.sem, 1)
                elif (stage, name) == ("M0", "xdbl"):
                    fill(b, s_xds, lag, 1)
                    pe.wait_ge(s_xs.sem, s_xs.at(k, 2))
                    for m in range(HALF):
                        last = nc.tensor.matmul(X[0:RK + 2 * NS, :], w_x[:, m, :], xs[:, m, :], start=(m == 0), stop=(m == 1))
                    last.then_inc(s_xd.sem, 1)
                elif (stage, name) == ("M0", "dt"):
                    m = a[0]
                    fill(b, s_rz, lag, m + 1)
                    pe.wait_ge(s_xds.sem, s_xds.at(k, 1))
                    nc.tensor.matmul(X[:, :], w_dt[:, m * P:(m + 1) * P], xdbl[0:RK, :], start=True, stop=True).then_inc(s_zt.sem, 1)
                elif (stage, name) == ("M1", "sum"):
                    c = a[0]
                    m = c % 2
                    if c < 2:
                        pe.wait_ge(s_y1.sem, s_y1.at(k, m - 1))
                    pe.wait_ge(s_ca.sem, s_ca.at(k, c + 1))
                    nc.tensor.matmul(Y[m][:, :], ident, bx[:, c % 3, 0, :], start=(c < 2), stop=(c >= NCH - 2)).then_inc(s_nr.sem, 1)
                elif (stage, name) == ("M2", "project"):
                    fill(b, s_t1, lag, 1)
                    pe.wait_ge(s_y2.sem, s_y2.at(k, 1))
                    for t in range(NT):
                        for m in range(HALF):
                            last = nc.tensor.matmul(X[:, t * P:(t + 1) * P], y[:, m, t * P:(t + 1) * P], w_out[:, m, :],
                                                    start=(m == 0), stop=(m == 1))
                    last.then_inc(s_po.sem, 1)
                elif (stage, name) == ("M2", "transpose"):
                    fill(b, s_hTn, lag, 2)
                    pe.wait_ge(s_xn2.sem, s_xn2.at(k, 4))
                    for t in range(NT):
                        last = nc.tensor.transpose(X[:, t * P:(t + 1) * P], xn[:, t, :], ident)
                    last.then_inc(s_T2.sem, 1)
                elif name == "gates":
                    fill(b, s_ga_sb, lag, a[0] + 1)
                    pe.wait_ge(s_hTn.sem, s_hTn.at(k, 2))
                    for j in range(2):
                        t = 2 * a[0] + j
                        last = nc.tensor.matmul(X[:, j * 256:(j + 1) * 256], hT2n[:, t * P:(t + 1) * P],
                                                wg_t[:, :, :, :].rearrange("p v e h -> p (v e h)"), start=True, stop=True)
                    last.then_inc(s_gt.sem, 1)
                elif name == "values":
                    t = a[0]
                    fill(b, s_ps, lag, t + 1)
                    nc.tensor.matmul(X[:, :], hT2n[:, t * P:(t + 1) * P], wv_t[:, :], start=True, stop=True).then_inc(s_pp.sem, 1)
                elif name == "mix":
                    rc, s = a
                    fill(b, s_v2, lag, 2 * rc + s + 1)
                    pe.wait_ge(s_p2.sem, s_p2.at(k, 1))
                    pe.wait_ge(s_bd.sem, s_bd.at(k, rc + 1))
                    for r in range(8):
                        last = nc.tensor.matmul(X[:, r * DH:(r + 1) * DH],
                                                bd[:, r, 8 * s:8 * s + 8, :].rearrange("p a h -> p (a h)"),
                                                P2[:, 8 * rc + r, :], start=True, stop=True)
                    last.then_inc(s_vm.sem, 1)
                elif name == "z":
                    s, j = a
                    fill(b, s_zs, lag, 4 * s + j + 1)
                    pe.wait_ge(s_A2.sem, s_A2.at(k, s + 1))
                    pe.wait_ge(s_bdo.sem, s_bdo.at(k, s + 1))
                    for r in range(8):
                        last = nc.tensor.matmul(X[0:DH, r * DH:(r + 1) * DH], A2b[:, 8 * j + r, :],
                                                bdo[:, 8 * j + r, :, :].rearrange("p k e -> p (k e)"), start=True, stop=True)
                    last.then_inc(s_z.sem, 1)
                elif name == "out":
                    s = a[0]
                    fill(b, s_o1, lag, s + 1)
                    pe.wait_ge(s_zs.sem, s_zs.at(k, 4 * s + 4))
                    for bb in range(2):
                        for e in range(NE):
                            last = nc.tensor.matmul(X[:, bb * P:(bb + 1) * P],
                                                    zT[:, 8 * e + 4 * bb:8 * e + 4 * bb + 4, :].rearrange("p g r -> p (g r)"),
                                                    wo_t[:, e, :], start=(e == 0), stop=(e == NE - 1))
                    last.then_inc(s_res.sem, 1)

            def project_q(k, n):
                s, h = divmod(2 * n, H)
                if n == 0:
                    pe.wait_ge(s_hT2.sem, s_hT2.at(k, 1))
                pe.wait_ge(s_qs.sem, s_qs.at(k, n))
                for j in range(2):
                    last = nc.tensor.matmul(Q[:, j * L:(j + 1) * L], m_qk[:, h + j, :], hT2[:, s * L:(s + 1) * L],
                                            start=True, stop=True)
                last.then_inc(s_q.sem, 1)

            def scores(k, i):
                s = i // H
                pe.wait_ge(s_qs.sem, s_qs.at(k, i // 2 + 1))
                pe.wait_ge(s_ex.sem, s_ex.at(k, i - 1))
                for it in range(2):
                    last = nc.tensor.matmul(S[i % 2][:, it * L:(it + 1) * L], qs[:, i // 2 % 2, i % 2, it * P:(it + 1) * P],
                                            hT2[:, s * L:(s + 1) * L], start=True, stop=True)
                last.then_inc(s_sc.sem, 1)

            def turn_probs(k, i):
                pe.wait_ge(s_ex.sem, s_ex.at(k, i + 1))
                pe.wait_ge(s_pt.sem, s_pt.at(k, i))
                for jt in range(2):
                    for it in range(2):
                        last = nc.tensor.transpose(PT[:, jt * L + it * P:jt * L + (it + 1) * P],
                                                   Pm[:, i % 2, it, jt * P:(jt + 1) * P], ident)
                last.then_inc(s_tp.sem, 1)

            def attend(k, i):
                s, h = divmod(i, H)
                if h == 0:
                    pe.wait_ge(s_v.sem, s_v.at(k, s + 1))
                if i % 4 == 0:
                    pe.wait_ge(s_oa.sem, s_oa.at(k, i // 4))
                pe.wait_ge(s_pt.sem, s_pt.at(k, i + 1))
                for it in range(2):
                    for jt in range(2):
                        o = ((h % 4) * 2 + it) * DH
                        last = nc.tensor.matmul(O[:, o:o + DH], PTs[:, i % 2, jt, it * P:(it + 1) * P],
                                                v[:, s, jt * H + h, :], start=(jt == 0), stop=(jt == 1))
                last.then_inc(s_pv.sem, 1)

            def body(b):
                k = b + LAG["A1"]
                heads = has("A1", b)
                if heads:
                    project_q(k, 0)
                    project_q(k, 1)
                    scores(k, 0)
                    scores(k, 1)
                for i in range(SLOTS):
                    if heads:
                        turn_probs(k, i)
                        if i + 2 < SLOTS:
                            scores(k, i + 2)
                    for stage, *a in steps("tensor", i):
                        if has(stage, b):
                            step(b, stage, *a)
                    if heads:
                        if i:
                            attend(k, i - 1)
                        if i % 2 == 0 and i + 4 < SLOTS:
                            project_q(k, i // 2 + 2)
                    for stage, *a in steps("tensor", i + 0.5):
                        if has(stage, b):
                            step(b, stage, *a)
                if heads:
                    attend(k, SLOTS - 1)
                s, lag, j = freed[0]
                freed[0] = (s, lag - 1, j)

            run(pe, body)

        @block.scalar
        def _(act):
            act.wait_ge(su_pe.sem, su_pe.at(0, 1))
            nc.scalar.activation(cT, X[:, 0:NSEQ], ACT.Copy).then_inc(su_act.sem, 1)
            act.wait_ge(w_small.sem, w_small.at(0, 16 * 18))
            nc.scalar.activation(a_neg[:, :, :], a_neg[:, :, :], ACT.Exp).then_inc(su_th.sem, 1)
            act.wait_ge(su_act.sem, su_act.at(0, 1))
            nc.scalar.activation(th_c, cT, ACT.Tanh, scale=0.5).then_inc(su_th.sem, 1)
            act.wait_ge(su_pe.sem, su_pe.at(0, 2))
            nc.scalar.activation(wv_t[:, :], X[:, :], ACT.Copy, scale=0.5).then_inc(su_act.sem, 1)
            act.wait_ge(su_pe.sem, su_pe.at(0, 3))
            nc.scalar.activation(wg_t[:, 0].rearrange("p e h -> p h e"), X[:, 0:P].rearrange("p (h e) -> p h e", e=NE), ACT.Copy)
            nc.scalar.activation(wg_t[:, 1].rearrange("p e h -> p h e"), X[:, P:2 * P].rearrange("p (h e) -> p h e", e=NE),
                                 ACT.Copy).then_inc(su_act.sem, 1)
            for i in range(2):
                act.wait_ge(su_pe.sem, su_pe.at(0, 4 + i))
                nc.scalar.activation(wo_t[:, 4 * i:4 * i + 4, :].rearrange("p e f -> p (e f)"), X[0:DH, :], ACT.Copy)\
                    .then_inc(su_act.sem, 1)
            for i in range(4):
                act.wait_ge(su_pe.sem, su_pe.at(0, 6 + i))
                nc.scalar.activation(m_qk[:, 4 * i:4 * i + 4, :].rearrange("p e f -> p (e f)"), X[:, :], ACT.Copy,
                                     scale=float(DH) ** -0.5).then_inc(su_act.sem, 1)
            act.wait_ge(su_pe.sem, su_pe.at(0, 10))
            nc.scalar.activation(mod_t[:, :, :].rearrange("p a n -> p (a n)"), X[:, 0:4 * NSEQ], ACT.Copy).then_inc(su_act.sem, 1)
            act.wait_ge(su_pe.sem, su_pe.at(0, 11))
            nc.scalar.activation(g_raw, X[0:NSEQ, 0:2 * DM], ACT.Copy).then_inc(su_act.sem, 1)
            act.wait_ge(su_dve.sem, su_dve.at(0, SETUP_DVE))

            def step(k, stage, name, *a):
                if (stage, name) == ("M0", "transpose"):
                    act.wait_ge(s_T1.sem, s_T1.at(k, 1))
                    act.wait_ge(s_cur1.sem, s_cur1.at(k, 1))
                    act.wait_ge(s_inp.sem, s_inp.at(k, 0))
                    for s in range(2):
                        nc.scalar.activation(hT[:, s * L:(s + 1) * L], X[:, s * L:(s + 1) * L], ACT.Identity,
                                             bias=cur1[:, 0, s:s + 1], scale=cur1[:, 1, s:s + 1]).then_inc(s_hT.sem, 1)
                elif (stage, name) == ("M0", "project"):
                    m = a[0]
                    act.wait_ge(s_inp.sem, s_inp.at(k, m + 1))
                    if m < 2:
                        act.wait_ge(s_cv.sem, s_cv.at(k, 4 * (m - 1)))
                        nc.scalar.activation(xcp[:, m, :, NCONV - 1:], X[:, :].rearrange("p (s t) -> p s t", s=2), ACT.Copy)\
                            .then_inc(s_xc.sem, 1)
                    else:
                        act.wait_ge(s_sres.sem, s_sres.at(k, m - 2))
                        nc.scalar.activation(thr_res[:, :], X[:, :], ACT.Tanh, scale=0.5).then_inc(s_thr.sem, 1)
                elif (stage, name) == ("M0", "conv"):
                    m = a[0]
                    act.wait_ge(s_cv.sem, s_cv.at(k, 4 * m + 4))
                    act.wait_ge(s_xs.sem, s_xs.at(k, m))
                    nc.scalar.activation(th_u[:, :], u[:, :], ACT.Tanh).then_inc(s_thu.sem, 1)
                elif (stage, name) == ("M0", "xdbl"):
                    act.wait_ge(s_xd.sem, s_xd.at(k, 1))
                    act.wait_ge(s_zt.sem, s_zt.at(k, 0))
                    act.wait_ge(s_bcw.sem, s_bcw.at(k, 0))
                    nc.scalar.activation(xdbl[:, :], X[0:RK + 2 * NS, :], ACT.Copy).then_inc(s_xds.sem, 1)
                elif (stage, name) == ("M0", "dt"):
                    m = a[0]
                    act.wait_ge(s_zt.sem, s_zt.at(k, m + 1))
                    if m == 0:
                        act.wait_ge(s_dt.sem, s_dt.at(k, 0))
                        if is_pair(k - 2):
                            act.wait_ge(s_mixT.sem, s_mixT.at(k - 2, 1))
                    nc.scalar.activation(lz[:, m, :], X[:, :], ACT.Abs, bias=bdt[:, m:m + 1]).then_inc(s_az.sem, 1)
                elif (stage, name) == ("M0", "log"):
                    act.wait_ge(s_az.sem, s_az.at(k, 2))
                    flat = lz[:, :, :].rearrange("p a t -> p (a t)")
                    nc.scalar.activation(flat, flat, ACT.Exp, scale=-1.0).then_inc(s_ez.sem, 1)
                    act.wait_ge(s_ez.sem, s_ez.at(k, 1))
                    nc.scalar.activation(flat, flat, ACT.Ln, bias=one).then_inc(s_lz.sem, 1)
                elif (stage, name) == ("M1", "chunk"):
                    c = a[0]
                    g, m = divmod(c, 2)
                    if c == 0:
                        act.wait_ge(s_dt.sem, s_dt.at(k, 1))
                    act.wait_ge(s_scan.sem, s_scan.at(k, c - 1))
                    for j in range(2):
                        last = nc.scalar.activation(dA[:, c % 2, j, :, 1:], dt2[:, m, :].rearrange("p (s t) -> p s t", s=2)[:, :, 1:],
                                                    ACT.Exp, scale=a_neg[:, m, 2 * g + j:2 * g + j + 1])
                    last.then_inc(s_dA.sem, 1)
                elif (stage, name) == ("M2", "transpose"):
                    act.wait_ge(s_T2.sem, s_T2.at(k, 1))
                    act.wait_ge(s_cur2.sem, s_cur2.at(k, 1))
                    if is_pair(k - 1):
                        act.wait_ge(s_hT2.sem, s_hT2.at(k - 1, 1))
                    act.wait_ge(s_pp.sem, s_pp.at(k, 0))
                    for s in range(2):
                        nc.scalar.activation(hT2n[:, s * L:(s + 1) * L], X[:, s * L:(s + 1) * L], ACT.Identity,
                                             bias=cur2[:, 0, s:s + 1], scale=cur2[:, 1, s:s + 1]).then_inc(s_hTn.sem, 1)
                elif name == "gates":
                    act.wait_ge(s_gt.sem, s_gt.at(k, a[0] + 1))
                    if a[0] == 0:
                        if is_pair(k + 1):
                            act.wait_ge(s_dt.sem, s_dt.at(k + 1, 1))
                    for j in range(2):
                        t = 2 * a[0] + j
                        for vo in range(2):
                            last = nc.scalar.activation(
                                gall[:, :, vo, t * H:(t + 1) * H],
                                X[:, j * 256 + vo * P:j * 256 + (vo + 1) * P].rearrange("p (e h) -> p e h", e=NE), ACT.Copy)
                    last.then_inc(s_ga_sb.sem, 1)
                elif name == "top2":
                    act.wait_ge(s_ga_sb.sem, s_ga_sb.at(k, 2))
                    nc.scalar.activation(thv, gall[:, :, 0, :], ACT.Tanh, scale=0.5).then_inc(s_thv.sem, 1)
                elif name == "values":
                    t = a[0]
                    act.wait_ge(s_pp.sem, s_pp.at(k, t + 1))
                    if t == 0:
                        if is_pair(k - 1):
                            act.wait_ge(s_v.sem, s_v.at(k - 1, 1))
                        act.wait_ge(s_p2.sem, s_p2.at(k, 0))
                    nc.scalar.activation(psb[:, t * 512:(t + 1) * 512], X[:, :], ACT.Copy).then_inc(s_ps.sem, 1)
                elif name == "mix":
                    rc, s = a
                    act.wait_ge(s_vm.sem, s_vm.at(k, 2 * rc + s + 1))
                    act.wait_ge(s_p2.sem, s_p2.at(k, 1))
                    if (rc, s) == (0, 1):
                        if is_pair(k - 1):
                            act.wait_ge(s_v.sem, s_v.at(k - 1, 2))
                    nc.scalar.activation(V2[:, s, 8 * rc:8 * rc + 8, :], X[:, :].rearrange("p (r d) -> p r d", r=8), ACT.Copy)\
                        .then_inc(s_v2.sem, 1)
                elif name == "z":
                    s, j = a
                    act.wait_ge(s_z.sem, s_z.at(k, 4 * s + j + 1))
                    if j == 0:
                        act.wait_ge(s_res.sem, s_res.at(k, s))
                        if is_pair(k + 1):
                            act.wait_ge(s_vm.sem, s_vm.at(k + 1, 8))
                    nc.scalar.activation(zT.rearrange("p (e g) r -> p r g e", e=NE)[:, 8 * j:8 * j + 8],
                                         X[0:DH, :].rearrange("p (r g e) -> p r g e", r=8, e=NE), ACT.Copy).then_inc(s_zs.sem, 1)

            def exps(k, i):
                s, h = divmod(i, H)
                act.wait_ge(s_mx.sem, s_mx.at(k, i + 1))
                act.wait_ge(s_tp.sem, s_tp.at(k, i - 1))
                if h == 0:
                    if is_pair(k - 1):
                        act.wait_ge(s_rl.sem, s_rl.at(k - 1, s + 1))
                for it in range(2):
                    last = nc.scalar.activation(Pm[:, i % 2, it, :], S[i % 2][:, it * L:(it + 1) * L], ACT.Exp,
                                                bias=nmax[:, i % 2, it:it + 1], accum_out=lsum[:, s, it, h:h + 1])
                last.then_inc(s_ex.sem, 1)

            def copy_probs(k, i):
                act.wait_ge(s_tp.sem, s_tp.at(k, i + 1))
                act.wait_ge(s_pv.sem, s_pv.at(k, i - 1))
                nc.scalar.activation(PTs[:, i % 2, :, :].rearrange("p j i -> p (j i)"), PT[:, :], ACT.Copy).then_inc(s_pt.sem, 1)

            def copy_attn(k, n):
                s, part = divmod(n, 4)
                act.wait_ge(s_pv.sem, s_pv.at(k, 4 * n + 4))
                if part == 0:
                    act.wait_ge(s_A2.sem, s_A2.at(k, s))
                nc.scalar.activation(attn[:, :, 4 * part:4 * part + 4, :],
                                     O[:, :].rearrange("p (h b d) -> p b h d", h=4, b=2), ACT.Copy).then_inc(s_oa.sem, 1)

            def hand_over(k):
                act.wait_ge(s_chosen.sem, s_chosen.at(k, 1))
                if is_pair(k - 1):
                    act.wait_ge(s_mo.sem, s_mo.at(k - 1, 1))
                    nc.scalar.activation(chosen_t[:, :, :], chosen_c[:, :, 2 * H:4 * H], ACT.Copy).then_inc(s_cht.sem, 1)
                    act.wait_ge(s_cht.sem, s_cht.at(k - 1, 1))
                nc.scalar.activation(chosen_c[:, :, :], chosen[:, :, 1, :], ACT.Copy).then_inc(s_chc.sem, 1)

            def body(b):
                k = b + LAG["A1"]
                heads = has("A1", b)
                if heads:
                    hand_over(k)
                    exps(k, 0)
                for i in range(SLOTS):
                    if heads and i + 1 < SLOTS:
                        exps(k, i + 1)
                    for stage, *a in steps("scalar", i):
                        if has(stage, b):
                            step(b + LAG[stage], stage, *a)
                    if heads:
                        copy_probs(k, i)
                        if i and i % 4 == 0:
                            copy_attn(k, i // 4 - 1)
                    for stage, *a in steps("scalar", i + 0.5):
                        if has(stage, b):
                            step(b + LAG[stage], stage, *a)
                if heads:
                    copy_attn(k, 7)

            run(act, body)

        @block.vector
        def _(dve):
            dve.wait_ge(w_small.sem, w_small.at(0, 16 * 18))
            n = [0]

            def setup(ins):
                ins.then_inc(su_dve.sem, 1)
                n[0] += 1
                return n[0]

            dve.wait_ge(su_th.sem, su_th.at(0, 2))
            setup(nc.vector.scalar_tensor_tensor(out=silu_c, in0=th_c, scalar=1.0, in1=cT, op0=ALU.add, op1=ALU.mult))
            setup(nc.vector.tensor_scalar(cw[:, :, :], cw[:, :, :], 0.5, None, ALU.mult))
            setup(nc.vector.tensor_scalar(cb[:, :], cb[:, :], 0.5, None, ALU.mult))
            setup(nc.vector.tensor_scalar(w_out[:, :, :], w_out[:, :, :], 0.5, None, ALU.mult))
            setup(nc.vector.tensor_scalar(a_neg[:, :, :], a_neg[:, :, :], -1.0, None, ALU.mult))
            dve.wait_ge(su_act.sem, su_act.at(0, 11))
            for i in range(4):
                setup(nc.vector.tensor_scalar(mod_t[:, i, :], mod_t[:, i, :], 0.5, float(i % 2), ALU.mult, ALU.add))
            a1 = setup(nc.vector.tensor_scalar(g_raw, g_raw, 0.5, None, ALU.mult))
            dve.wait_ge(su_dve.sem, su_dve.at(0, a1))
            a2 = setup(nc.vector.tensor_scalar(g_sign, g_raw, 0.0, 2.0, ALU.is_ge, ALU.mult))
            a2 = setup(nc.vector.tensor_scalar(g_abs, g_raw, -1.0, 0.25, ALU.mult, ALU.max))
            dve.wait_ge(su_dve.sem, su_dve.at(0, a2))
            a3 = setup(nc.vector.tensor_tensor(g_raw, g_raw, g_abs, ALU.max))
            dve.wait_ge(su_dve.sem, su_dve.at(0, a3))
            nc.vector.scalar_tensor_tensor(out=gate_rows.rearrange("n g c -> n (g c)"), in0=g_sign, scalar=-1.0, in1=g_raw,
                                           op0=ALU.add, op1=ALU.mult).then_inc(su_gate.sem, 1)
            setup(nc.vector.memset(xcp[:, :, :, 0:NCONV - 1], 0.0))
            setup(nc.vector.memset(dA[:, :, :, :, 0:1], 0.0))
            dve.wait_ge(su_pool.sem, su_pool.at(0, 16))
            assert n[0] == SETUP_DVE, n[0]

            def token_stats(k, src, st, mv, ve, cur, part, s_st, s_mv, s_ve, s_cur, s_hn):
                for t in range(NT):
                    nc.vector.bn_stats(st[:, t, :], src[:, t, :]).then_inc(s_st.sem, 1)
                dve.wait_ge(s_st.sem, s_st.at(k, 4))
                dve.wait_ge(s_hn.sem, s_hn.at(k, 0))
                nc.vector.tensor_copy(cur[:, :, :], mod_t[:, part:part + 2, bass.ds(2 * k, 2)]).then_inc(s_cur.sem, 1)
                for t in range(NT):
                    nc.vector.bn_aggr(mv[:, t, :], st[:, t, :]).then_inc(s_mv.sem, 1)
                dve.wait_ge(s_mv.sem, s_mv.at(k, 4))
                nc.vector.tensor_scalar(ve[:, :], mv[:, :, 1], EPS, None, ALU.add).then_inc(s_ve.sem, 1)

            def normalise(k, src, mv, rs, part, s_rs, s_dst, s_turned):
                dve.wait_ge(s_rs.sem, s_rs.at(k, 1))
                if part == 0:
                    if is_pair(k - 2):
                        dve.wait_ge(s_T2.sem, s_T2.at(k - 2, 1))
                elif is_pair(k + 1):
                    dve.wait_ge(s_T1.sem, s_T1.at(k + 1, 1))
                dve.wait_ge(s_turned.sem, s_turned.at(k, 0))
                for t in range(NT):
                    nc.vector.tensor_scalar(xn[:, t, :], src[:, t, :], mv[:, t, 0:1], rs[:, t:t + 1], ALU.subtract, ALU.mult)\
                        .then_inc(s_dst.sem, 1)

            def step(k, stage, name, *a):
                if (stage, name) == ("M0", "norm"):
                    dve.wait_ge(s_xa.sem, s_xa.at(k, 16))
                    token_stats(k, xa, stat, mv1, ve1, cur1, 0, s_st1, s_mv1, s_ve1, s_cur1, s_hT)
                elif (stage, name) == ("M0", "scale"):
                    normalise(k, xa, mv1, rs1, 0, s_rs1, s_xn, s_T1)
                elif (stage, name) == ("M0", "project"):
                    m = a[0] - 2
                    if m >= 0:
                        dve.wait_ge(s_thr.sem, s_thr.at(k, m + 1))
                        dve.wait_ge(s_sr2.sem, s_sr2.at(k, 0))
                        nc.vector.scalar_tensor_tensor(out=sres1[:, m, :], in0=thr_res[:, :], scalar=1.0, in1=X[:, :],
                                                       op0=ALU.add, op1=ALU.mult).then_inc(s_sres.sem, 1)
                elif (stage, name) == ("M0", "conv"):
                    m = a[0]
                    dve.wait_ge(s_xc.sem, s_xc.at(k, m + 1))
                    dve.wait_ge(s_xs.sem, s_xs.at(k, m))
                    u3 = u[:, :].rearrange("p (s t) -> p s t", s=2)
                    nc.vector.tensor_scalar(u3, xcp[:, m, :, 0:L], cw[:, m, 0:1], cb[:, m:m + 1], ALU.mult, ALU.add)\
                        .then_inc(s_cv.sem, 1)
                    for j in range(1, NCONV):
                        dve.wait_ge(s_cv.sem, s_cv.at(k, 4 * m + j))
                        nc.vector.scalar_tensor_tensor(out=u3, in0=xcp[:, m, :, j:j + L], scalar=cw[:, m, j:j + 1], in1=u3,
                                                       op0=ALU.mult, op1=ALU.add).then_inc(s_cv.sem, 1)
                    dve.wait_ge(s_thu.sem, s_thu.at(k, m + 1))
                    if m == 0:
                        dve.wait_ge(s_xd.sem, s_xd.at(k, 0))
                        dve.wait_ge(s_y0.sem, s_y0.at(k, 0))
                    nc.vector.scalar_tensor_tensor(out=xs[:, m, :], in0=th_u[:, :], scalar=1.0, in1=u[:, :],
                                                   op0=ALU.add, op1=ALU.mult).then_inc(s_xs.sem, 1)
                elif (stage, name) == ("M0", "dt"):
                    m = a[0]
                    dve.wait_ge(s_az.sem, s_az.at(k, m + 1))
                    nc.vector.tensor_scalar(rz[:, m, :], X[:, :], bdt[:, m:m + 1], 0.0, ALU.add, ALU.max).then_inc(s_rz.sem, 1)
                elif (stage, name) == ("M1", "start"):
                    dve.wait_ge(s_lz.sem, s_lz.at(k, 1))
                    dve.wait_ge(s_rz.sem, s_rz.at(k, 2))
                    dve.wait_ge(s_dA.sem, s_dA.at(k, 0))
                    nc.vector.tensor_tensor(dt2[:, :, :], rz[:, :, :], lz[:, :, :], ALU.add).then_inc(s_dt.sem, 1)
                    dve.wait_ge(s_po.sem, s_po.at(k, 0))
                    for m in range(HALF):
                        nc.vector.tensor_scalar(y[:, m, :], xs[:, m, :], d_skip[:, m:m + 1], None, ALU.mult).then_inc(s_y0.sem, 1)
                    dve.wait_ge(s_dt.sem, s_dt.at(k, 1))
                    dve.wait_ge(s_bm.sem, s_bm.at(k, 0))
                    dve.wait_ge(s_bcw.sem, s_bcw.at(k, 16))
                    nc.vector.tensor_tensor(dtx[:, :, :], dt2[:, :, :], xs[:, :, :], ALU.mult).then_inc(s_dtx.sem, 1)
                    nc.vector.tensor_copy(sres2[:, :, :], sres1[:, :, :]).then_inc(s_sr2.sem, 1)
                elif (stage, name) == ("M1", "chunk"):
                    c = a[0]
                    dve.wait_ge(s_dA.sem, s_dA.at(k, c + 1))
                    dve.wait_ge(s_bm.sem, s_bm.at(k, c + 1))
                    flat = bx[:, c % 3, :, :].rearrange("p j t -> p (j t)")
                    nc.vector.tensor_tensor_scan(flat, dA[:, c % 2].rearrange("p j s t -> p (j s t)"), flat, 0.0,
                                                 ALU.mult, ALU.add).then_inc(s_scan.sem, 1)
                elif (stage, name) == ("M2", "gate"):
                    dve.wait_ge(s_nr.sem, s_nr.at(k, NCH))
                    dve.wait_ge(s_y0.sem, s_y0.at(k, 2))
                    for m in range(HALF):
                        nc.vector.tensor_tensor(y[:, m, :], y[:, m, :], Y[m][:, :], ALU.add).then_inc(s_y1.sem, 1)
                    dve.wait_ge(s_y1.sem, s_y1.at(k, 2))
                    dve.wait_ge(s_sr2.sem, s_sr2.at(k, 1))
                    nc.vector.tensor_tensor(y[:, :, :], y[:, :, :], sres2[:, :, :], ALU.mult).then_inc(s_y2.sem, 1)
                elif (stage, name) == ("M2", "residual"):
                    dve.wait_ge(s_po.sem, s_po.at(k, 1))
                    dve.wait_ge(s_ga.sem, s_ga.at(k, 16))
                    dve.wait_ge(s_x1w.sem, s_x1w.at(k, 0))
                    nc.vector.tensor_tensor(x1[:, :, :].rearrange("p (s b) c -> p s b c", s=2),
                                            X[:, :].rearrange("p (s b c) -> p s b c", s=2, b=2),
                                            grow(ga[:, :, :], 2, 2), ALU.mult).then_inc(s_t1.sem, 1)
                    dve.wait_ge(s_xb.sem, s_xb.at(k, 16))
                    dve.wait_ge(s_t1.sem, s_t1.at(k, 1))
                    nc.vector.tensor_tensor(x1[:, :, :], x1[:, :, :], xb[:, :, :], ALU.add).then_inc(s_x1.sem, 1)
                    dve.wait_ge(s_x1.sem, s_x1.at(k, 1))
                    token_stats(k, x1, stat2, mv2, ve2, cur2, 2, s_st2, s_mv2, s_ve2, s_cur2, s_hTn)
                elif (stage, name) == ("M2", "scale"):
                    normalise(k, x1, mv2, rs2, 2, s_rs2, s_xn2, s_T2)
                elif name == "rank":
                    d = a[0]
                    done = 3 * d - 2
                    g3 = gall[:, :, :, :].rearrange("p e v n -> p e (v n)")
                    if d == 1:
                        dve.wait_ge(s_ga_sb.sem, s_ga_sb.at(k, 2))
                        nc.vector.memset(score[:, :, :], 0.0).then_inc(s_score.sem, 1)
                    dve.wait_ge(s_score.sem, s_score.at(k, done))
                    nc.vector.tensor_tensor(beats[:, 0:NE - d, :], g3[:, 0:NE - d, :], g3[:, d:NE, :], ALU.is_ge)\
                        .then_inc(s_score.sem, 1)
                    dve.wait_ge(s_score.sem, s_score.at(k, done + 1))
                    nc.vector.tensor_tensor(score[:, 0:NE - d, :], score[:, 0:NE - d, :], beats[:, 0:NE - d, :], ALU.add)\
                        .then_inc(s_score.sem, 1)
                    dve.wait_ge(s_score.sem, s_score.at(k, done + 2))
                    nc.vector.tensor_tensor(score[:, d:NE, :], score[:, d:NE, :], beats[:, 0:NE - d, :], ALU.subtract)\
                        .then_inc(s_score.sem, 1)
                elif name == "top2":
                    dve.wait_ge(s_score.sem, s_score.at(k, 3 * NE - 2))
                    if is_pair(k - 1):
                        dve.wait_ge(s_chc.sem, s_chc.at(k - 1, 1))
                    nc.vector.tensor_tensor(chosen[:, :, :, :].rearrange("p e v n -> p e (v n)"), score[:, :, :],
                                            grow(thr, 2, P), ALU.is_ge).then_inc(s_chosen.sem, 1)
                    dve.wait_ge(s_thv.sem, s_thv.at(k, 1))
                    nc.vector.tensor_scalar(thv, thv, 1.0, None, ALU.add).then_inc(s_sg.sem, 1)
                    dve.wait_ge(s_chosen.sem, s_chosen.at(k, 1))
                    dve.wait_ge(s_sg.sem, s_sg.at(k, 1))
                    nc.vector.tensor_tensor(mixn.rearrange("p t e h -> p e t h"),
                                            thv.rearrange("p e (t h) -> p e t h", t=NT),
                                            chosen[:, :, 0, :].rearrange("p e (t h) -> p e t h", t=NT), ALU.mult)\
                        .then_inc(s_mix.sem, 1)
                elif (stage, name) == ("A0", "turn"):
                    dve.wait_ge(s_ps.sem, s_ps.at(k, 4))
                    dve.wait_ge(s_vm.sem, s_vm.at(k, 0))
                    if is_pair(k - 2):
                        dve.wait_ge(s_res.sem, s_res.at(k - 2, 2))
                    nc.vector.transpose(P2[:, :, :].rearrange("p r d -> p d r"), psb.rearrange("p (g d) -> p d g", d=DH))\
                        .then_inc(s_p2.sem, 1)
                    dve.wait_ge(s_mix.sem, s_mix.at(k, 1))
                    nc.vector.transpose(mixT[:, :, :].rearrange("p r h -> p h r"),
                                        mixn.rearrange("p t e h -> p h (t e)")).then_inc(s_mixT.sem, 1)
                elif name == "attn":
                    s = a[0]
                    dve.wait_ge(s_ex.sem, s_ex.at(k, H * s + H))
                    nc.vector.reciprocal(rl[:, :], lsum[:, s, :, :].rearrange("p b h -> p (b h)")).then_inc(s_rl.sem, 1)
                    dve.wait_ge(s_rl.sem, s_rl.at(k, s + 1))
                    if s == 0:
                        dve.wait_ge(s_chc.sem, s_chc.at(k, 1))
                        ch = chosen_c[:, :, 0:2 * H]
                    else:
                        moved = is_pair(k + 1)
                        if moved:
                            dve.wait_ge(s_cht.sem, s_cht.at(k, 1))
                        ch = chosen_t[:, :, :] if moved else chosen_c[:, :, 2 * H:4 * H]
                    nc.vector.tensor_tensor(mo[:, :, :], ch, grow(rl[:, :], 1, NE), ALU.mult).then_inc(s_mo.sem, 1)
                    dve.wait_ge(s_mo.sem, s_mo.at(k, s + 1))
                    nc.vector.transpose(moT[:, :, :].rearrange("p r e -> p e r"), mo[:, :, :]).then_inc(s_moT.sem, 1)
                elif name == "turn":
                    s = a[0]
                    dve.wait_ge(s_oa.sem, s_oa.at(k, 4 * s + 4))
                    dve.wait_ge(s_z.sem, s_z.at(k, 4 * s))
                    nc.vector.transpose(A2b[:, :, :].rearrange("p r d -> p d r"),
                                        attn[:, :, :, :].rearrange("p b h d -> p d (b h)")).then_inc(s_A2.sem, 1)
                elif name == "out":
                    s = a[0]
                    dve.wait_ge(s_res.sem, s_res.at(k, s + 1))
                    dve.wait_ge(s_gb.sem, s_gb.at(k, 16 * (s + 1)))
                    dve.wait_ge(s_out.sem, s_out.at(k, 16 * s))
                    nc.vector.tensor_tensor(ob[:, :, :], X[:, 0:2 * DM].rearrange("p (b c) -> p b c", b=2),
                                            grow(gb[:, :], 1, 2), ALU.mult).then_inc(s_o1.sem, 1)
                    dve.wait_ge(s_o1.sem, s_o1.at(k, s + 1))
                    dve.wait_ge(s_xr.sem, s_xr.at(k, 16 * (s + 1)))
                    nc.vector.tensor_tensor(ob[:, :, :], ob[:, :, :], xr[:, :, :], ALU.add).then_inc(s_ob.sem, 1)

            def hand_over(k):
                dve.wait_ge(s_hTn.sem, s_hTn.at(k, 2))
                dve.wait_ge(s_sc.sem, s_sc.at(k, 0))
                nc.vector.tensor_copy(hT2[:, :], hT2n[:, :]).then_inc(s_hT2.sem, 1)

            def turn_values(k, s):
                dve.wait_ge(s_v2.sem, s_v2.at(k, 8))
                dve.wait_ge(s_pv.sem, s_pv.at(k, 0))
                nc.vector.transpose(v[:, s, :, :].rearrange("p g d -> p d g"),
                                    V2[:, s, :, :].rearrange("p r d -> p d r")).then_inc(s_v.sem, 1)

            def copy_q(k, n):
                dve.wait_ge(s_q.sem, s_q.at(k, n + 1))
                dve.wait_ge(s_sc.sem, s_sc.at(k, 2 * n - 2))
                nc.vector.tensor_copy(qs[:, n % 2, :, :].rearrange("p j t -> p (j t)"), Q[:, :]).then_inc(s_qs.sem, 1)

            def row_max(k, i):
                dve.wait_ge(s_sc.sem, s_sc.at(k, i + 1))
                dve.wait_ge(s_ex.sem, s_ex.at(k, i - 1))
                nc.vector.tensor_reduce(nmax[:, i % 2, :], S[i % 2][:, :].rearrange("p (i j) -> p i j", i=2), AX.X, ALU.max,
                                        negate=True).then_inc(s_mx.sem, 1)

            def body(b):
                k = b + LAG["A1"]
                heads = has("A1", b)
                if heads:
                    hand_over(k)
                    copy_q(k, 0)
                    copy_q(k, 1)
                    row_max(k, 0)
                    row_max(k, 1)
                for i in range(SLOTS):
                    if heads:
                        if i + 2 < SLOTS:
                            row_max(k, i + 2)
                        if i % 2 and i + 3 < SLOTS:
                            copy_q(k, i // 2 + 2)
                    for stage, *a in steps("vector", i):
                        if has(stage, b):
                            step(b + LAG[stage], stage, *a)
                    if heads and i in (0, 9):
                        turn_values(k, i // 9)
                    for stage, *a in steps("vector", i + 0.5):
                        if has(stage, b):
                            step(b + LAG[stage], stage, *a)

            run(dve, body)

        @block.gpsimd
        def _(pool):
            pool.wait_ge(su_dve.sem, su_dve.at(0, SETUP_DVE))

            def step(k, stage, name, *a):
                if (stage, name) in (("M0", "norm"), ("M2", "residual")):
                    ve, rs, s_ve, s_rs, s_xn_ = (ve1, rs1, s_ve1, s_rs1, s_xn) if stage == "M0" else (ve2, rs2, s_ve2, s_rs2, s_xn2)
                    pool.wait_ge(s_ve.sem, s_ve.at(k, 1))
                    pool.wait_ge(s_xn_.sem, s_xn_.at(k, 0))
                    nc.gpsimd.tensor_tensor(rs[:, :], ve[:, :], minus_half.to_broadcast([P, NT]), ALU.pow).then_inc(s_rs.sem, 1)
                elif (stage, name) == ("M1", "chunk"):
                    c = a[0]
                    g, m = divmod(c, 2)
                    if c == 0:
                        pool.wait_ge(s_dtx.sem, s_dtx.at(k, 1))
                    pool.wait_ge(s_bb[g % 2].sem, s_bb[g % 2].at(k, 16 * (g // 2 + 1)))
                    pool.wait_ge(s_nr.sem, s_nr.at(k, max(c - 2, 0)))
                    nc.gpsimd.tensor_tensor(bx[:, c % 3], grow(dtx[:, m, :], 1, 2), Bb[:, g % 2], ALU.mult).then_inc(s_bm.sem, 1)
                elif (stage, name) == ("A0", "spread"):
                    rc = a[0]
                    pool.wait_ge(s_mixT.sem, s_mixT.at(k, 1))
                    pool.wait_ge(s_vm.sem, s_vm.at(k, 2 * rc))
                    if rc == 0:
                        if is_pair(k - 2):
                            pool.wait_ge(s_z.sem, s_z.at(k - 2, 8))
                    nc.gpsimd.tensor_tensor(bd[:, :, :, :], grow(mixT[:, 8 * rc:8 * rc + 8, :], 2, 16),
                                            grow(grow(mask_v, 1, 8), 3, H), ALU.mult).then_inc(s_bd.sem, 1)
                elif name == "spread":
                    s = a[0]
                    pool.wait_ge(s_z.sem, s_z.at(k, 4 * s))
                    if s == 0:
                        if is_pair(k + 1):
                            pool.wait_ge(s_vm.sem, s_vm.at(k + 1, 8))
                    pool.wait_ge(s_moT.sem, s_moT.at(k, s + 1))
                    nc.gpsimd.tensor_tensor(bdo[:, :, :, :], grow(moT[:, :, :], 2, 8), grow(grow(mask_o, 1, 32), 3, NE),
                                            ALU.mult).then_inc(s_bdo.sem, 1)
                elif (stage, name) == ("M1", "times_c"):
                    c = a[0]
                    g = c // 2
                    pool.wait_ge(s_scan.sem, s_scan.at(k, c + 1))
                    pool.wait_ge(s_cb[g % 2].sem, s_cb[g % 2].at(k, 16 * (g // 2 + 1)))
                    nc.gpsimd.tensor_tensor(bx[:, c % 3], bx[:, c % 3], Cb[:, g % 2], ALU.mult).then_inc(s_cm.sem, 1)
                    pool.wait_ge(s_cm.sem, s_cm.at(k, c + 1))
                    nc.gpsimd.tensor_tensor(bx[:, c % 3, 0], bx[:, c % 3, 0], bx[:, c % 3, 1], ALU.add).then_inc(s_ca.sem, 1)

            def body(b):
                for i in range(2 * SLOTS):
                    for stage, *a in steps("gpsimd", i / 2):
                        if has(stage, b):
                            step(b + LAG[stage], stage, *a)

            run(pool, body)


_INS = ["L0_attn_x", "L0_attn_W_in", "L0_attn_conv_w", "L0_attn_conv_b", "L0_attn_W_x", "L0_attn_W_dt", "L0_attn_b_dt",
        "L0_attn_A_log", "L0_attn_D", "L0_attn_W_out", "L0_ffn_Wq", "L0_ffn_Wk", "L0_ffn_Wv", "L0_ffn_Ws", "L0_ffn_Wd",
        "L0_ffn_Wo", "L0_c", "L0_wmod"]


def kernel(**inputs):
    import concourse.bacc as bacc
    from concourse.bass_utils import run_bass_kernel_spmd

    nc = bacc.Bacc("TRN2", target_bir_lowering=False, num_devices=1)
    arrays, args = {}, []
    for name in _INS:
        a = np.ascontiguousarray(inputs[name])
        arrays[f"in_{name}"] = a
        args.append(nc.dram_tensor(f"in_{name}", a.shape, mybir.dt.from_np(a.dtype), kind="ExternalInput").ap())
    shape_only = constants()
    arrays["in_constants"] = shape_only
    args.append(nc.dram_tensor("in_constants", shape_only.shape, F32, kind="ExternalInput").ap())
    out = nc.dram_tensor("out_x", (NSEQ, L, DM), F32, kind="ExternalOutput").ap()
    build(nc, *args, out)
    r = run_bass_kernel_spmd(nc, [arrays], core_ids=[0])
    return r.results[0]["out_x"]
```
